# Optimizing a Trainium2 kernel written in Bass

```python
import numpy as np
import jax
import jax.numpy as jnp

def _softmax(x, axis=-1):
    return jax.nn.softmax(x, axis=axis)
def _gelu(x):
    return jax.nn.gelu(x, approximate=True)
def _silu(x):
    return jax.nn.silu(x)
def _sigmoid(x):
    return jax.nn.sigmoid(x)
def _layernorm(x, axis=-1, eps=1e-5):
    m = jnp.mean(x, axis=axis, keepdims=True)
    v = jnp.var(x, axis=axis, keepdims=True)
    return (x - m) / jnp.sqrt(v + eps)
def _scatter_add(tgt, idx, src, axis=0):
    return tgt.at[idx].add(src)
def _segment_sum(src, seg, n):
    return jax.ops.segment_sum(src, seg, n)

kernel_name = 'mk_rec_standalone_d1_rec_0fc071'

def setup_inputs(seed: int = 0):
    np.random.seed(seed)
    _w = jnp.asarray
    def _rec_inputs():
        import jax
        import jax.numpy as jnp
        _rk = jax.random.key(seed)
        r_x = jnp.stack([jax.random.randint(jax.random.fold_in(jax.random.fold_in(_rk, 1), 0), (16384,), 2, 26000, jnp.int32), jax.random.randint(jax.random.fold_in(jax.random.fold_in(_rk, 1), 1), (16384,), 1, 25996, jnp.int32), jax.random.randint(jax.random.fold_in(jax.random.fold_in(_rk, 1), 2), (16384,), 2, 26000, jnp.int32), jax.random.randint(jax.random.fold_in(jax.random.fold_in(_rk, 1), 3), (16384,), 1, 25998, jnp.int32), jax.random.randint(jax.random.fold_in(jax.random.fold_in(_rk, 1), 4), (16384,), 1, 25996, jnp.int32), jax.random.randint(jax.random.fold_in(jax.random.fold_in(_rk, 1), 5), (16384,), 2, 25999, jnp.int32), jax.random.randint(jax.random.fold_in(jax.random.fold_in(_rk, 1), 6), (16384,), 5, 25999, jnp.int32), jax.random.randint(jax.random.fold_in(jax.random.fold_in(_rk, 1), 7), (16384,), 0, 25998, jnp.int32), jax.random.randint(jax.random.fold_in(jax.random.fold_in(_rk, 1), 8), (16384,), 0, 26000, jnp.int32), jax.random.randint(jax.random.fold_in(jax.random.fold_in(_rk, 1), 9), (16384,), 1, 25993, jnp.int32), jax.random.randint(jax.random.fold_in(jax.random.fold_in(_rk, 1), 10), (16384,), 4, 25998, jnp.int32), jax.random.randint(jax.random.fold_in(jax.random.fold_in(_rk, 1), 11), (16384,), 0, 26000, jnp.int32), jax.random.randint(jax.random.fold_in(jax.random.fold_in(_rk, 1), 12), (16384,), 0, 26000, jnp.int32), jax.random.randint(jax.random.fold_in(jax.random.fold_in(_rk, 1), 13), (16384,), 3, 26000, jnp.int32), jax.random.randint(jax.random.fold_in(jax.random.fold_in(_rk, 1), 14), (16384,), 1, 25997, jnp.int32), jax.random.randint(jax.random.fold_in(jax.random.fold_in(_rk, 1), 15), (16384,), 0, 25999, jnp.int32), jax.random.randint(jax.random.fold_in(jax.random.fold_in(_rk, 1), 16), (16384,), 1, 25997, jnp.int32), jax.random.randint(jax.random.fold_in(jax.random.fold_in(_rk, 1), 17), (16384,), 0, 26000, jnp.int32), jax.random.randint(jax.random.fold_in(jax.random.fold_in(_rk, 1), 18), (16384,), 0, 25999, jnp.int32), jax.random.randint(jax.random.fold_in(jax.random.fold_in(_rk, 1), 19), (16384,), 0, 25999, jnp.int32), jax.random.randint(jax.random.fold_in(jax.random.fold_in(_rk, 1), 20), (16384,), 0, 25999, jnp.int32), jax.random.randint(jax.random.fold_in(jax.random.fold_in(_rk, 1), 21), (16384,), 1, 26000, jnp.int32), jax.random.randint(jax.random.fold_in(jax.random.fold_in(_rk, 1), 22), (16384,), 0, 25999, jnp.int32), jax.random.randint(jax.random.fold_in(jax.random.fold_in(_rk, 1), 23), (16384,), 0, 25998, jnp.int32), jax.random.randint(jax.random.fold_in(jax.random.fold_in(_rk, 1), 24), (16384,), 1, 25999, jnp.int32), jax.random.randint(jax.random.fold_in(jax.random.fold_in(_rk, 1), 25), (16384,), 1, 25999, jnp.int32), jax.random.randint(jax.random.fold_in(jax.random.fold_in(_rk, 1), 26), (16384,), 2, 26000, jnp.int32), jax.random.randint(jax.random.fold_in(jax.random.fold_in(_rk, 1), 27), (16384,), 4, 26000, jnp.int32), jax.random.randint(jax.random.fold_in(jax.random.fold_in(_rk, 1), 28), (16384,), 0, 26000, jnp.int32), jax.random.randint(jax.random.fold_in(jax.random.fold_in(_rk, 1), 29), (16384,), 0, 26000, jnp.int32), jax.random.randint(jax.random.fold_in(jax.random.fold_in(_rk, 1), 30), (16384,), 0, 26000, jnp.int32), jax.random.randint(jax.random.fold_in(jax.random.fold_in(_rk, 1), 31), (16384,), 2, 25998, jnp.int32), jax.random.randint(jax.random.fold_in(jax.random.fold_in(_rk, 1), 32), (16384,), 2, 26000, jnp.int32), jax.random.randint(jax.random.fold_in(jax.random.fold_in(_rk, 1), 33), (16384,), 0, 26000, jnp.int32), jax.random.randint(jax.random.fold_in(jax.random.fold_in(_rk, 1), 34), (16384,), 3, 25999, jnp.int32), jax.random.randint(jax.random.fold_in(jax.random.fold_in(_rk, 1), 35), (16384,), 1, 25999, jnp.int32), jax.random.randint(jax.random.fold_in(jax.random.fold_in(_rk, 1), 36), (16384,), 1, 26000, jnp.int32), jax.random.randint(jax.random.fold_in(jax.random.fold_in(_rk, 1), 37), (16384,), 2, 25998, jnp.int32), jax.random.randint(jax.random.fold_in(jax.random.fold_in(_rk, 1), 38), (16384,), 0, 26000, jnp.int32)], axis=1)
        return r_x
    r_x = _rec_inputs()
    def _L0_rec_setup():
        import jax, jax.numpy as jnp
        import numpy as np
        FIELD_DIMS = [26000] * 39
        EMBED_DIM = 64
        MLP_DIMS = [400, 400, 400]
        BATCH = 16384
        OFFSETS = jnp.asarray(np.concatenate(([0], np.cumsum(FIELD_DIMS)[:-1])), dtype=jnp.int32)
        BN_INV = 1.0 / np.sqrt(1.0 + 1e-05)
        key = jax.random.key(seed)
        ks = jax.random.split(key, 16)
        B, F, E = (BATCH, len(FIELD_DIMS), EMBED_DIM)
        V = sum(FIELD_DIMS)
        s = lambda k, shp, sc=0.05: jax.random.normal(k, shp, jnp.float32) * sc
        inp = {'x': jax.random.randint(ks[0], (B, F), 0, FIELD_DIMS[0], dtype=jnp.int32), 'emb_table': s(ks[1], (V, E)), 'lin_table': s(ks[2], (V, 1)), 'lin_bias': jnp.zeros((1,), jnp.float32), 'sparse_var': s(ks[3], (F, E), 0.1), 'Wt': s(ks[4], (F, E, E)), 'bt': jnp.zeros((F, E), jnp.float32)}
        dims = [F * E] + MLP_DIMS
        for i in range(3):
            inp[f'W{i + 1}'] = s(ks[5 + i], (dims[i], dims[i + 1]))
            inp[f'b{i + 1}'] = jnp.zeros((dims[i + 1],), jnp.float32)
            inp[f'g{i + 1}'] = jnp.ones((dims[i + 1],), jnp.float32)
            inp[f'be{i + 1}'] = jnp.zeros((dims[i + 1],), jnp.float32)
        inp['Wout'] = s(ks[9], (MLP_DIMS[-1], 1))
        inp['bout'] = jnp.zeros((1,), jnp.float32)
        return inp
    _L0_rec_all = _L0_rec_setup()
    _L0_rec_in = {k: v for k, v in _L0_rec_all.items() if k in ('emb_table', 'lin_table', 'lin_bias', 'sparse_var', 'Wt', 'bt', 'W1', 'b1', 'g1', 'be1', 'W2', 'b2', 'g2', 'be2', 'W3', 'b3', 'g3', 'be3', 'Wout', 'bout', )}
    del _L0_rec_all

    return {
        "r_x": r_x,
        "L0_rec_emb_table": _L0_rec_in["emb_table"],
        "L0_rec_lin_table": _L0_rec_in["lin_table"],
        "L0_rec_lin_bias": _L0_rec_in["lin_bias"],
        "L0_rec_sparse_var": _L0_rec_in["sparse_var"],
        "L0_rec_Wt": _L0_rec_in["Wt"],
        "L0_rec_bt": _L0_rec_in["bt"],
        "L0_rec_W1": _L0_rec_in["W1"],
        "L0_rec_b1": _L0_rec_in["b1"],
        "L0_rec_g1": _L0_rec_in["g1"],
        "L0_rec_be1": _L0_rec_in["be1"],
        "L0_rec_W2": _L0_rec_in["W2"],
        "L0_rec_b2": _L0_rec_in["b2"],
        "L0_rec_g2": _L0_rec_in["g2"],
        "L0_rec_be2": _L0_rec_in["be2"],
        "L0_rec_W3": _L0_rec_in["W3"],
        "L0_rec_b3": _L0_rec_in["b3"],
        "L0_rec_g3": _L0_rec_in["g3"],
        "L0_rec_be3": _L0_rec_in["be3"],
        "L0_rec_Wout": _L0_rec_in["Wout"],
        "L0_rec_bout": _L0_rec_in["bout"],
    }

def reference(r_x, L0_rec_emb_table, L0_rec_lin_table, L0_rec_lin_bias, L0_rec_sparse_var, L0_rec_Wt, L0_rec_bt, L0_rec_W1, L0_rec_b1, L0_rec_g1, L0_rec_be1, L0_rec_W2, L0_rec_b2, L0_rec_g2, L0_rec_be2, L0_rec_W3, L0_rec_b3, L0_rec_g3, L0_rec_be3, L0_rec_Wout, L0_rec_bout):
    import jax
    import jax.numpy as jnp
    def _L0_rec_ref(x, emb_table, lin_table, lin_bias, sparse_var, Wt, bt, W1, b1, g1, be1, W2, b2, g2, be2, W3, b3, g3, be3, Wout, bout):
        import jax, jax.numpy as jnp
        import numpy as np
        FIELD_DIMS = [26000] * 39
        EMBED_DIM = 64
        MLP_DIMS = [400, 400, 400]
        BATCH = 16384
        OFFSETS = jnp.asarray(np.concatenate(([0], np.cumsum(FIELD_DIMS)[:-1])), dtype=jnp.int32)
        BN_INV = 1.0 / np.sqrt(1.0 + 1e-05)
        B = x.shape[0]
        idx = x + OFFSETS[None, :]
        sv = jax.nn.sigmoid(jax.lax.stop_gradient(sparse_var) * 15.0)
        sv = jnp.where(sv > 0.001, sv, 0.0)
        embed_x = emb_table[idx] * sv
        trans = jnp.einsum('bfi,foi->bfo', embed_x, Wt) + bt
        sum_f = trans.sum(axis=1)
        fm = 0.5 * jnp.sum(sum_f * sum_f - (trans * trans).sum(axis=1), axis=-1, keepdims=True)
        lin = lin_table[idx].sum(axis=1) + lin_bias
        h = embed_x.reshape(B, -1)
        for W, b, g, be in ((W1, b1, g1, be1), (W2, b2, g2, be2), (W3, b3, g3, be3)):
            h = jax.nn.relu((h @ W + b) * (BN_INV * g) + be)
        mlp = h @ Wout + bout
        return jax.nn.sigmoid(jnp.squeeze(lin + fm + mlp, axis=1))

    y = _L0_rec_ref(r_x, L0_rec_emb_table, L0_rec_lin_table, L0_rec_lin_bias, L0_rec_sparse_var, L0_rec_Wt, L0_rec_bt, L0_rec_W1, L0_rec_b1, L0_rec_g1, L0_rec_be1, L0_rec_W2, L0_rec_b2, L0_rec_g2, L0_rec_be2, L0_rec_W3, L0_rec_b3, L0_rec_g3, L0_rec_be3, L0_rec_Wout, L0_rec_bout)
    return y


_drawn_inputs = setup_inputs


def setup_inputs(seed=0):
    import zlib

    import numpy as np

    out = dict(_drawn_inputs(seed))
    spreads = {'L0_rec_bt': (0.0, 0.1),
     'L0_rec_b1': (0.0, 0.1),
     'L0_rec_g1': (1.0, 0.6),
     'L0_rec_be1': (0.0, 0.537),
     'L0_rec_b2': (0.0, 0.691),
     'L0_rec_g2': (1.0, 0.6),
     'L0_rec_be2': (0.0, 0.541),
     'L0_rec_b3': (0.0, 0.427),
     'L0_rec_g3': (1.0, 0.6),
     'L0_rec_be3': (0.0, 0.8)}
    factors = {'L0_rec_W1': 3.102, 'L0_rec_Wout': 3.324}
    for name, (base, spread) in spreads.items():
        noise = np.random.default_rng([zlib.crc32(name.encode()), seed]).standard_normal(out[name].shape)
        drawn = base * np.exp(spread * noise) if base else spread * noise
        out[name] = jnp.asarray(drawn.astype(out[name].dtype))
    for name, factor in factors.items():
        out[name] = (out[name] * factor).astype(out[name].dtype)
    return out
```

```python
import concourse.bass as bass
from concourse import mybir
from contextlib import ExitStack

F32 = mybir.dt.float32
I32 = mybir.dt.int32
ALU = mybir.AluOpType
ACT = mybir.ActivationFunctionType
AX = mybir.AxisListType

P = 128
F = 39
E = 64
EW = E + 1
H = 400
LAYERS = 3
H1 = H + E
PAIRS = 20
FP = 2 * PAIRS
CHUNKS = 5
CP = PAIRS // CHUNKS
CF = 2 * CP
KH = 100
HK = H // KH
BN_INV = 1.0 / (1.0 + 1e-05) ** 0.5
HW_FIELD = F - 1
REGS = 32
ACT_BLOCK = P // REGS - 1
LIN, TSQ, SSQ, MLP, PARTS = 0, CHUNKS, 2 * CHUNKS, 2 * CHUNKS + 1, 2 * CHUNKS + 2
C_ID, C_OFF, C_COEF, C_END = 0, P, P + F, P + F + PARTS


def fields_of(c):
    return range(CF * c, min(CF * (c + 1), F))


def deepfm_kernel(nc, table, rx, rx_hw, consts, gate, w1, wt, bt, w2, w3, gain, bias, beta, wout, scalars, out):
    TILES = rx.shape[1] // F
    PAIR_LOOPS = (TILES - 2) // 2
    FIELD_ROWS = table.shape[0] // F
    assert TILES % 2 == 0 and TILES >= 6

    ctx = ExitStack()
    with ctx:
        def sb(name, shape, dt=F32):
            return ctx.enter_context(nc.sbuf_tensor(name, shape, dt))

        def pb(name, shape):
            return ctx.enter_context(nc.psum_tensor(name, shape, F32))

        def sem(name):
            return ctx.enter_context(nc.semaphore(name))

        rx_sb = sb("rx_sb", [P, (TILES + 2) * F], I32)
        index = sb("index", [P, 2, F], I32)
        rows = sb("rows", [P, 2, PAIRS, 2 * EW])
        const_sb = sb("const_sb", [P, C_END])
        gate_raw = sb("gate_raw", [P, PAIRS])
        gate_sig = sb("gate_sig", [P, PAIRS])
        gate_sb = sb("gate_sb", [P, PAIRS])
        w1_sb = sb("w1_sb", [P, PAIRS, H1])
        wt_sb = sb("wt_sb", [P, PAIRS, P])
        bt_sb = sb("bt_sb", [P, FP * E])
        w23_sb = sb("w23_sb", [KH, 2, HK, H])
        gain_raw = sb("gain_raw", [P, LAYERS, H])
        bias_raw = sb("bias_raw", [P, LAYERS, H])
        beta_raw = sb("beta_raw", [P, LAYERS, H])
        scale_sb = sb("scale_sb", [P, LAYERS, H1])
        shift_sb = sb("shift_sb", [P, LAYERS, H1])
        shift_part = sb("shift_part", [P, LAYERS, H])
        wout_sb = sb("wout_sb", [P, H])
        scalars_sb = sb("scalars_sb", [P, 2])
        out_bias = sb("out_bias", [P, 1])
        xT = sb("xT", [P, 2, CP, P])
        z = sb("z", [P, H1])
        hT = sb("hT", [KH, HK, P])
        parts = sb("parts", [P, 2, PARTS])
        weighed = sb("weighed", [P, PARTS])
        logit = sb("logit", [P, 1])
        logits = sb("logits", [P, TILES])
        probs = sb("probs", [P, TILES])

        x_ps = [pb(f"x_ps{i}", [P, CP, P]) for i in range(2)]
        t_ps = [pb(f"t_ps{i}", [P, CP * P]) for i in range(2)]
        h_ps = [pb(f"h_ps{i}", [P, 512]) for i in range(2)]
        y_ps = pb("y_ps", [P, 512])
        zT_ps = pb("zT_ps", [P, HK, P])

        identity = const_sb[:, C_ID:C_ID + P]
        offsets = const_sb[:, C_OFF:C_OFF + F]
        coefs = const_sb[:, C_COEF:C_COEF + PARTS]

        first_idx_in = sem("first_idx_in")
        const_in = sem("const_in")
        rest_idx_in = sem("rest_idx_in")
        gate_in = sem("gate_in")
        w1_in = [sem(f"w1_in{c}") for c in range(CHUNKS)]
        wt_in = sem("wt_in")
        bt_in = sem("bt_in")
        w23_in = sem("w23_in")
        affine_in = sem("affine_in")
        out_in = sem("out_in")
        rows_in = [[sem(f"rows_in{s}_{c}") for c in range(CHUNKS)] for s in range(2)]
        hw_rows_in = sem("hw_rows_in")
        stored = sem("stored")
        first_index = sem("first_index")
        pads_zeroed = sem("pads_zeroed")
        gate_sig_done = sem("gate_sig_done")
        gate_done = sem("gate_done")
        setup_step = sem("setup_step")
        gather_ready = sem("gather_ready")
        gathers_begun = sem("gathers_begun")
        fetches_begun = sem("fetches_begun")
        rows_transposed = sem("rows_transposed")
        xT_ready = sem("xT_ready")
        lin_summed = sem("lin_summed")
        chunk_multiplied = sem("chunk_multiplied")
        t_biased = sem("t_biased")
        t_squared = sem("t_squared")
        z_scaled = sem("z_scaled")
        z_ready = sem("z_ready")
        sum_squared = sem("sum_squared")
        z_transposed = sem("z_transposed")
        hT_ready = sem("hT_ready")
        y_ready = sem("y_ready")
        mlp_ready = sem("mlp_ready")
        logit_ready = sem("logit_ready")
        logit_stored = sem("logit_stored")
        probs_ready = sem("probs_ready")

        def load_indices(eng, regs, odd, b):
            eng.load(regs, rx_hw[bass.ds(odd, 1), REGS * b:REGS * (b + 1)])

        def fetch_rows(eng, regs, b, js):
            for j in js:
                at = eng.snap(regs[j], min_val=0, max_val=FIELD_ROWS - 1)
                p = REGS * b + j
                eng.dma_start(rows[p:p + 1, 1, HW_FIELD // 2, 0:EW],
                              table[bass.ds(at + HW_FIELD * FIELD_ROWS, 1), :]).then_inc(hw_rows_in, 16)

        block = ctx.enter_context(nc.Block())

        @block.sync
        def _(sp):
            sp.dma_start(rx_sb[:, 0:2 * F], rx[:, 0:2 * F]).then_inc(first_idx_in, 16)
            sp.dma_start(gate_raw[:, :], gate).then_inc(gate_in, 16)
            for c in range(CHUNKS):
                sp.dma_start(w1_sb[:, CP * c:CP * (c + 1), :], w1[:, CP * c:CP * (c + 1), :]).then_inc(w1_in[c], 16)
                if c == 0:
                    sp.dma_start(wt_sb[:, :, :], wt).then_inc(wt_in, 16)
            sp.dma_start(rx_sb[:, 2 * F:TILES * F], rx[:, 2 * F:TILES * F]).then_inc(rest_idx_in, 16)
            regs = [sp.alloc_register(f"sp_index{j}") for j in range(REGS)]
            for b in range(ACT_BLOCK):
                load_indices(sp, regs, 0, b)
                fetch_rows(sp, regs, b, range(REGS))
            with sp.Fori(0, PAIR_LOOPS) as i:
                sp.wait_ge(gather_ready, (i + 1) * (2 * CHUNKS))
                sp.sem_inc(fetches_begun, 1)
                for b in range(ACT_BLOCK):
                    load_indices(sp, regs, i + 1, b)
                    fetch_rows(sp, regs, b, range(REGS))
            sp.wait_ge(probs_ready, 1)
            sp.dma_start(out.rearrange("(p t) -> p t", t=TILES), probs[:, :]).then_inc(stored, 16)
            sp.wait_ge(stored, 16)

        @block.gpsimd
        def _(pool):
            def gather(slot, c):
                for f in fields_of(c):
                    if slot == 1 and f == HW_FIELD:
                        continue
                    pool.indirect_dma_start(
                        rows[:, slot, f // 2, f % 2 * EW:(f % 2 + 1) * EW], None, table,
                        bass.IndirectOffsetOnAxis(ap=index[:, slot, f:f + 1], axis=0),
                    ).then_inc(rows_in[slot][c], 16)

            pool.wait_ge(first_index, 1)
            for slot in range(2):
                for c in range(CHUNKS):
                    gather(slot, c)
            with pool.Fori(0, TILES // 2 - 1) as i:
                for slot in range(2):
                    for c in range(CHUNKS):
                        pool.wait_ge(gather_ready, i * (2 * CHUNKS) + slot * CHUNKS + c + 1)
                        pool.sem_inc(gathers_begun, 1)
                        gather(slot, c)

        @block.tensor
        def _(pe):
            def transpose_rows(uses, slot, c):
                n = len(fields_of(c))
                if slot == 1 and c == CHUNKS - 1:
                    pe.wait_ge(hw_rows_in, uses * (16 * P))
                    n -= 1
                pe.wait_ge(rows_in[slot][c], uses * (16 * n))
                bank = x_ps[(slot * CHUNKS + c) % 2]
                for j in range(CP):
                    k = CP * c + j
                    last = nc.tensor.transpose(bank[:, j, :], rows[:, slot, k, 1:1 + 2 * E], identity)
                last.then_inc(rows_transposed, 1)

            def multiply(t, slot, c, first=False):
                buf = (slot * CHUNKS + c) % 2
                pe.wait_ge(xT_ready, t * CHUNKS + c + 1)
                if not (first and c < 2):
                    pe.wait_ge(t_squared, t * CHUNKS + c - 1)
                for j in range(CP):
                    k = CP * c + j
                    nc.tensor.matmul(h_ps[slot][:, 0:H1], xT[:, buf, j, :], w1_sb[:, k, :],
                                     start=(k == 0), stop=(k == PAIRS - 1))
                    last = nc.tensor.matmul(t_ps[buf][:, P * j:P * (j + 1)], xT[:, buf, j, :],
                                            wt_sb[:, k, :], start=True, stop=True)
                last.then_inc(chunk_multiplied, 1)

            def transpose_z(t, layer):
                pe.wait_ge(z_ready, t * LAYERS + layer + 1)
                for j in range(HK):
                    last = nc.tensor.transpose(zT_ps[0:KH, j, :], z[:, KH * j:KH * (j + 1)], identity)
                last.then_inc(z_transposed, 1)

            def hidden(t, layer):
                pe.wait_ge(hT_ready, t * 2 + layer + 1)
                for j in range(HK):
                    last = nc.tensor.matmul(y_ps[:, 0:H], hT[:, j, :], w23_sb[:, layer, j, :],
                                            start=(j == 0), stop=(j == HK - 1))
                last.then_inc(y_ready, 1)

            def tile(t, slot, uses):
                transpose_rows(uses, slot, 0)
                multiply(t, slot, 0)
                transpose_rows(uses, slot, 1)
                transpose_z(t - 1, 0)
                multiply(t, slot, 1)
                transpose_rows(uses, slot, 2)
                hidden(t - 1, 0)
                multiply(t, slot, 2)
                transpose_rows(uses, slot, 3)
                transpose_z(t - 1, 1)
                multiply(t, slot, 3)
                transpose_rows(uses, slot, 4)
                hidden(t - 1, 1)
                multiply(t, slot, 4)

            pe.wait_ge(const_in, 16)
            pe.wait_ge(pads_zeroed, 1)
            for c in range(CHUNKS):
                transpose_rows(1, 0, c)
                if c == 0:
                    pe.wait_ge(wt_in, 16)
                pe.wait_ge(w1_in[c], 16)
                multiply(0, 0, c, first=True)
            pe.wait_ge(w23_in, 32)
            with pe.Fori(0, PAIR_LOOPS) as i:
                tile(i * 2 + 1, 1, i + 1)
                tile(i * 2 + 2, 0, i + 2)
            tile(TILES - 1, 1, TILES // 2)
            for layer in range(2):
                transpose_z(TILES - 1, layer)
                hidden(TILES - 1, layer)

        @block.vector
        def _(dve):
            def scale_x(t, slot, c):
                buf = (slot * CHUNKS + c) % 2
                dve.wait_ge(rows_transposed, t * CHUNKS + c + 1)
                g = gate_sb[:, CP * c:CP * (c + 1)].unsqueeze(2).to_broadcast([P, CP, P])
                nc.vector.tensor_tensor(xT[:, buf, :, :], x_ps[buf][:, :, :], g, ALU.mult).then_inc(xT_ready, 1)

            def add_bt(t, slot, c):
                buf = (slot * CHUNKS + c) % 2
                dve.wait_ge(chunk_multiplied, t * CHUNKS + c + 1)
                nc.vector.tensor_tensor(t_ps[buf][:, :], t_ps[buf][:, :], bt_sb[:, CP * P * c:CP * P * (c + 1)],
                                        ALU.add).then_inc(t_biased, 1)

            def sum_lin(t, slot, c):
                nc.vector.tensor_reduce(parts[:, slot, LIN + c:LIN + c + 1],
                                        rows[:, slot, CP * c:CP * (c + 1), 0:2 * EW:2 * EW - 1],
                                        AX.XY, ALU.add).then_inc(lin_summed, 1)

            def next_index(t, slot, c):
                fs = fields_of(c)
                src = (t + 2) * F + fs[0]
                dve.wait_ge(lin_summed, t * CHUNKS + c + 1)
                nc.vector.tensor_tensor(index[:, slot, fs[0]:fs[-1] + 1], rx_sb[:, bass.ds(src, len(fs))],
                                        offsets[:, fs[0]:fs[-1] + 1], ALU.add).then_inc(gather_ready, 1)

            def affine(t, layer, ps, width, to):
                nc.vector.tensor_tensor(ps, ps, scale_sb[:, layer, 0:width], ALU.mult).then_inc(z_scaled, 1)
                dve.wait_ge(z_scaled, t * LAYERS + layer + 1)
                nc.vector.tensor_tensor(to, ps, shift_sb[:, layer, 0:width], ALU.add).then_inc(z_ready, 1)

            def affine_2(t):
                dve.wait_ge(y_ready, t * 2 + 1)
                affine(t, 1, y_ps[:, 0:H], H, z[:, 0:H])

            def finish(t, slot):
                dve.wait_ge(y_ready, t * 2 + 2)
                affine(t, 2, y_ps[:, 0:H], H, y_ps[:, 0:H])
                dve.wait_ge(z_ready, t * LAYERS + 3)
                nc.vector.scalar_tensor_tensor(y_ps[:, 0:H], y_ps[:, 0:H], 0.0, wout_sb[:, :], ALU.max, ALU.mult,
                                               accum_out=parts[:, slot, MLP:MLP + 1]).then_inc(mlp_ready, 1)
                dve.wait_ge(t_squared, (t + 1) * CHUNKS)
                dve.wait_ge(sum_squared, t + 1)
                dve.wait_ge(mlp_ready, t + 1)
                nc.vector.scalar_tensor_tensor(weighed[:, :], parts[:, slot, :], 1.0, coefs, ALU.mult, ALU.mult,
                                               accum_out=logit[:, :]).then_inc(logit_ready, 1)
                dve.wait_ge(logit_ready, t + 1)
                nc.vector.tensor_copy(logits[:, bass.ds(t, 1)], logit[:, :]).then_inc(logit_stored, 1)

            def tile(t, slot):
                scale_x(t, slot, 0)
                add_bt(t - 1, 1 - slot, CHUNKS - 1)
                affine(t - 1, 0, h_ps[1 - slot][:, 0:H1], H1, z[:, :])
                sum_lin(t, slot, 0)
                next_index(t, slot, 0)
                for c in range(1, CHUNKS):
                    scale_x(t, slot, c)
                    add_bt(t, slot, c - 1)
                    sum_lin(t, slot, c)
                    next_index(t, slot, c)
                    if c == 2:
                        affine_2(t - 1)
                    if c == 4:
                        finish(t - 1, 1 - slot)

            dve.wait_ge(first_idx_in, 16)
            dve.wait_ge(const_in, 16)
            nc.vector.tensor_tensor(index[:, :, :], rx_sb[:, 0:2 * F].rearrange("p (s f) -> p s f", s=2),
                                    offsets.unsqueeze(1).to_broadcast([P, 2, F]), ALU.add).then_inc(first_index, 1)
            nc.vector.memset(rows[:, :, PAIRS - 1, EW:2 * EW], 0.0).then_inc(pads_zeroed, 1)
            nc.vector.memset(rx_sb[:, TILES * F:(TILES + 2) * F], 0)
            nc.vector.memset(scale_sb[:, 0, H:H1], 1.0)
            dve.wait_ge(gate_sig_done, 1)
            nc.vector.scalar_tensor_tensor(gate_sb[:, :], gate_sig[:, :], 0.001, gate_sig[:, :],
                                           ALU.is_gt, ALU.mult).then_inc(gate_done, 1)
            dve.wait_ge(bt_in, 16)
            nc.vector.tensor_reduce(shift_sb[:, 0, H:H1], bt_sb[:, :].rearrange("p (f o) -> p o f", o=E),
                                    AX.X, ALU.add)
            dve.wait_ge(affine_in, 48)
            nc.vector.tensor_scalar(scale_sb[:, :, 0:H], gain_raw[:, :, :], BN_INV, None,
                                    ALU.mult).then_inc(setup_step, 1)
            dve.wait_ge(setup_step, 1)
            nc.vector.tensor_tensor(shift_part[:, :, :], bias_raw[:, :, :], scale_sb[:, :, 0:H],
                                    ALU.mult).then_inc(setup_step, 1)
            dve.wait_ge(setup_step, 2)
            nc.vector.tensor_tensor(shift_sb[:, :, 0:H], shift_part[:, :, :], beta_raw[:, :, :],
                                    ALU.add).then_inc(setup_step, 1)
            dve.wait_ge(out_in, 32)
            nc.vector.tensor_tensor(out_bias[:, :], scalars_sb[:, 0:1], scalars_sb[:, 1:2],
                                    ALU.add).then_inc(setup_step, 1)
            dve.wait_ge(setup_step, 4)
            dve.wait_ge(gate_done, 1)
            dve.wait_ge(rest_idx_in, 16)

            for c in range(CHUNKS):
                scale_x(0, 0, c)
                if c:
                    add_bt(0, 0, c - 1)
                sum_lin(0, 0, c)
                next_index(0, 0, c)
            with dve.Fori(0, PAIR_LOOPS) as i:
                tile(i * 2 + 1, 1)
                tile(i * 2 + 2, 0)
            tile(TILES - 1, 1)
            dve.wait_ge(chunk_multiplied, TILES * CHUNKS)
            affine(TILES - 1, 0, h_ps[1][:, 0:H1], H1, z[:, :])
            add_bt(TILES - 1, 1, CHUNKS - 1)
            affine_2(TILES - 1)
            finish(TILES - 1, 1)

        @block.scalar
        def _(act):
            def square_t(t, slot, c):
                act.wait_ge(t_biased, t * CHUNKS + c + 1)
                ps = t_ps[(slot * CHUNKS + c) % 2]
                nc.scalar.activation(ps[:, :], ps[:, :], ACT.Square,
                                     accum_out=parts[:, slot, TSQ + c:TSQ + c + 1]).then_inc(t_squared, 1)

            def square_sum(t, slot):
                act.wait_ge(z_ready, t * LAYERS + 1)
                nc.scalar.activation(z[:, H:H1], z[:, H:H1], ACT.Square,
                                     accum_out=parts[:, slot, SSQ:SSQ + 1]).then_inc(sum_squared, 1)

            def relu(t, layer):
                act.wait_ge(z_transposed, t * 2 + layer + 1)
                nc.scalar.activation(hT[:, :, :], zT_ps[0:KH, :, :], ACT.Relu).then_inc(hT_ready, 1)

            regs = [act.alloc_register(f"act_index{j}") for j in range(REGS)]

            def fetch_quarter(odd, q):
                if q == 0:
                    load_indices(act, regs, odd, ACT_BLOCK)
                fetch_rows(act, regs, ACT_BLOCK, range(REGS // 4 * q, REGS // 4 * (q + 1)))

            def tile(t, slot, odd=None):
                square_t(t - 1, 1 - slot, CHUNKS - 1)
                square_sum(t - 1, 1 - slot)
                square_t(t, slot, 0)
                if odd is not None:
                    act.wait_ge(gather_ready, t * CHUNKS)
                    act.sem_inc(fetches_begun, 1)
                    fetch_quarter(odd, 0)
                relu(t - 1, 0)
                square_t(t, slot, 1)
                if odd is not None:
                    fetch_quarter(odd, 1)
                square_t(t, slot, 2)
                if odd is not None:
                    fetch_quarter(odd, 2)
                relu(t - 1, 1)
                square_t(t, slot, 3)
                if odd is not None:
                    fetch_quarter(odd, 3)

            act.dma_start(const_sb[:, :], consts).then_inc(const_in, 16)
            act.dma_start(bt_sb[:, :], bt.partition_broadcast(P)).then_inc(bt_in, 16)
            act.dma_start(gain_raw[:, :, :], gain.partition_broadcast(P)).then_inc(affine_in, 16)
            act.dma_start(bias_raw[:, :, :], bias.partition_broadcast(P)).then_inc(affine_in, 16)
            act.dma_start(beta_raw[:, :, :], beta.partition_broadcast(P)).then_inc(affine_in, 16)
            act.dma_start(scalars_sb[:, :], scalars.partition_broadcast(P)).then_inc(out_in, 16)
            act.dma_start(wout_sb[:, :], wout.partition_broadcast(P)).then_inc(out_in, 16)
            act.dma_start(w23_sb[:, 0, :, :], w2.rearrange("(k p) n -> p k n", p=KH)).then_inc(w23_in, 16)
            act.dma_start(w23_sb[:, 1, :, :], w3.rearrange("(k p) n -> p k n", p=KH)).then_inc(w23_in, 16)
            act.wait_ge(gate_in, 16)
            nc.scalar.activation(gate_sig[:, :], gate_raw[:, :], ACT.Sigmoid, scale=15.0).then_inc(gate_sig_done, 1)

            for q in range(4):
                fetch_quarter(0, q)
            for c in range(CHUNKS - 1):
                square_t(0, 0, c)
            with act.Fori(0, PAIR_LOOPS) as i:
                tile(i * 2 + 1, 1)
                tile(i * 2 + 2, 0, odd=i + 1)
            tile(TILES - 1, 1)
            relu(TILES - 1, 0)
            square_sum(TILES - 1, 1)
            square_t(TILES - 1, 1, CHUNKS - 1)
            relu(TILES - 1, 1)
            act.wait_ge(logit_stored, TILES)
            nc.scalar.activation(probs[:, :], logits[:, :], ACT.Sigmoid, bias=out_bias[:, :]).then_inc(probs_ready, 1)


def kernel(r_x, L0_rec_emb_table, L0_rec_lin_table, L0_rec_lin_bias, L0_rec_sparse_var, L0_rec_Wt, L0_rec_bt,
           L0_rec_W1, L0_rec_b1, L0_rec_g1, L0_rec_be1, L0_rec_W2, L0_rec_b2, L0_rec_g2, L0_rec_be2,
           L0_rec_W3, L0_rec_b3, L0_rec_g3, L0_rec_be3, L0_rec_Wout, L0_rec_bout):
    import numpy as np
    import concourse.bacc as bacc
    from concourse.bass_utils import run_bass_kernel_spmd

    asnp = np.asarray
    B = r_x.shape[0]
    V = L0_rec_emb_table.shape[0]

    emb = asnp(L0_rec_emb_table).reshape(F, V // F, E)
    lin = asnp(L0_rec_lin_table).reshape(F, V // F, 1)
    table = np.empty((F, V // F, EW), np.float32)
    table[0::2, :, 0:1], table[0::2, :, 1:] = lin[0::2], emb[0::2]
    table[1::2, :, :E], table[1::2, :, E:] = emb[1::2], lin[1::2]
    table = table.reshape(V, EW)
    consts = np.zeros((P, C_END), np.float32)
    consts[:, C_ID:C_ID + P] = np.eye(P, dtype=np.float32)
    consts[:, C_OFF:C_OFF + F] = np.arange(F, dtype=np.float32) * (V // F)
    consts[:, C_COEF + LIN:C_COEF + LIN + CHUNKS] = 1.0
    consts[:, C_COEF + TSQ:C_COEF + TSQ + CHUNKS] = -0.5
    consts[:, C_COEF + SSQ] = 0.5
    consts[:, C_COEF + MLP] = 1.0
    gate = np.zeros((FP, E), np.float32)
    gate[:F] = asnp(L0_rec_sparse_var)
    gate = gate.reshape(PAIRS, P).T
    wtT = asnp(L0_rec_Wt).transpose(0, 2, 1)
    w1 = np.zeros((FP * E, H1), np.float32)
    w1[:F * E, :H] = asnp(L0_rec_W1)
    w1[:F * E, H:] = wtT.reshape(F * E, E)
    w1 = w1.reshape(PAIRS, P, H1).transpose(1, 0, 2)
    wt = np.zeros((PAIRS, P, P), np.float32)
    for f in range(F):
        s = slice((f % 2) * E, (f % 2 + 1) * E)
        wt[f // 2, s, s] = wtT[f]
    wt = wt.transpose(1, 0, 2)
    bt = np.zeros((FP * E,), np.float32)
    bt[:F * E] = asnp(L0_rec_bt).reshape(-1)

    arrays = {
        "table": table,
        "rx": asnp(r_x).reshape(P, (B // P) * F),
        "rx_hw": asnp(r_x).reshape(P, B // P, F)[:, 1::2, HW_FIELD].T,
        "consts": consts,
        "gate": gate,
        "w1": w1,
        "wt": wt,
        "bt": bt,
        "w2": asnp(L0_rec_W2),
        "w3": asnp(L0_rec_W3),
        "gain": np.stack([asnp(L0_rec_g1), asnp(L0_rec_g2), asnp(L0_rec_g3)]),
        "bias": np.stack([asnp(L0_rec_b1), asnp(L0_rec_b2), asnp(L0_rec_b3)]),
        "beta": np.stack([asnp(L0_rec_be1), asnp(L0_rec_be2), asnp(L0_rec_be3)]),
        "wout": asnp(L0_rec_Wout).reshape(-1),
        "scalars": np.concatenate([asnp(L0_rec_lin_bias), asnp(L0_rec_bout)]),
    }
    arrays = {n: np.ascontiguousarray(a) for n, a in arrays.items()}
    nc = bacc.Bacc("TRN2", target_bir_lowering=False, num_devices=1)
    args = [nc.dram_tensor(n, a.shape, mybir.dt.from_np(a.dtype), kind="ExternalInput").ap()
            for n, a in arrays.items()]
    out = nc.dram_tensor("out", (B,), F32, kind="ExternalOutput").ap()
    deepfm_kernel(nc, *args, out)
    r = run_bass_kernel_spmd(nc, [arrays], core_ids=[0])
    return r.results[0]["out"]
```
